# Optimizing a Trainium2 kernel written in Bass

```python
import numpy as np
import jax
import jax.numpy as jnp

def _softmax(x, axis=-1):
    return jax.nn.softmax(x, axis=axis)

def _gelu(x):
    return jax.nn.gelu(x, approximate=True)

def _silu(x):
    return jax.nn.silu(x)

def _sigmoid(x):
    return jax.nn.sigmoid(x)

def _layernorm(x, axis=-1, eps=1e-05):
    m = jnp.mean(x, axis=axis, keepdims=True)
    v = jnp.var(x, axis=axis, keepdims=True)
    return (x - m) / jnp.sqrt(v + eps)

def _scatter_add(tgt, idx, src, axis=0):
    return tgt.at[idx].add(src)

def _segment_sum(src, seg, n):
    return jax.ops.segment_sum(src, seg, n)
kernel_name = 'mk_flamingo_gated_d1_seqx_r4_fa5512'

def setup_inputs(seed: int=0):
    np.random.seed(seed)
    _w = jnp.asarray

    def _rec_inputs():
        import jax
        import jax.numpy as jnp
        _rk = jax.random.key(seed)
        x = -0.0003929 + 0.9999 * jax.random.normal(jax.random.fold_in(_rk, 1), (64, 256, 256), jnp.float32)
        _lenS = 256 - jax.random.randint(jax.random.fold_in(_rk, 7), (64,), 0, max(1, 256 // 4) + 1, jnp.int32)
        _lenS2 = 77 - jax.random.randint(jax.random.fold_in(_rk, 8), (64,), 0, max(1, 77 // 4) + 1, jnp.int32)
        _ctx_1024P = jax.random.normal(jax.random.fold_in(_rk, 11), (64, 16, 256), jnp.float32)
        _ctx_1024c = jax.random.dirichlet(jax.random.fold_in(_rk, 511), 0.3 * jnp.ones((16,), jnp.float32), (64, 77))
        _ctx_1024t = jnp.einsum('bsk,bkd->bsd', _ctx_1024c, _ctx_1024P)
        _ctx_1024t = _ctx_1024t * jax.lax.rsqrt(jnp.mean(jnp.square(_ctx_1024t)) + 1e-12) * 0.953939
        ctx_1024 = 2.81802e-05 + 1.00001 * (_ctx_1024t + 0.3 * jax.random.normal(jax.random.fold_in(_rk, 611), (64, 77, 256), jnp.float32))
        _validS = jnp.arange(256)[None, :] < _lenS[:, None]
        _validS2 = jnp.arange(77)[None, :] < _lenS2[:, None]
        _causal = jnp.tril(jnp.ones((256, 256), dtype=bool))
        mask_BxSxS2_ik0 = jnp.where(jnp.broadcast_to(_validS2[:, None, :], (64, 256, 77)), 0, 1).astype(jnp.int32)
        _g = jax.random.normal(jax.random.fold_in(_rk, 9001), (2, 1), jnp.float32)
        _g = jnp.sign(_g) * jnp.maximum(jnp.abs(_g), 1.0) + (_g == 0) * 1.0
        g_xattn = _g[0]
        g_ffn = _g[1]
        return (x, ctx_1024, mask_BxSxS2_ik0, g_xattn, g_ffn)
    x, ctx_1024, mask_BxSxS2_ik0, g_xattn, g_ffn = _rec_inputs()

    def _L0_xattn_setup():
        import jax, jax.numpy as jnp
        import numpy as np
        NEG = -1000000000.0
        key = jax.random.key(seed)
        k1, k2, k3, k4 = jax.random.split(key, 4)
        B, Sq, Sk, D = (8, 512, 512, 256)
        query = jax.random.normal(k1, (B, Sq, D), dtype=jnp.float32)
        memories = jax.random.normal(k2, (B, Sk, D), dtype=jnp.float32)
        mask = jax.random.randint(k3, (B, Sq, Sk), 0, 2).astype(jnp.int32)
        W = jax.random.normal(k4, (D, D), dtype=jnp.float32) * (1.0 / np.sqrt(D))
        b = jnp.zeros((D,), dtype=jnp.float32)
        return {'query': query, 'memories': memories, 'mask': mask, 'W': W, 'b': b}
    _L0_xattn_all = _L0_xattn_setup()
    _L0_xattn_in = {k: v for k, v in _L0_xattn_all.items() if k in ('W', 'b')}
    del _L0_xattn_all

    def _L0_ffn_setup():
        import jax, jax.numpy as jnp
        import numpy as np
        key = jax.random.key(seed)
        kx, kw = jax.random.split(key)
        x = jax.random.normal(kx, (32, 1024, 256), dtype=jnp.float32)
        weight = jax.random.normal(kw, (256, 256), dtype=jnp.float32) * 0.01
        return {'x': x, 'weight': weight}
    _L0_ffn_all = _L0_ffn_setup()
    _L0_ffn_in = {k: v for k, v in _L0_ffn_all.items() if k in ('weight',)}
    del _L0_ffn_all
    return {'x': x, 'ctx_1024': ctx_1024, 'mask_BxSxS2_ik0': mask_BxSxS2_ik0, 'g_xattn': g_xattn, 'g_ffn': g_ffn, 'L0_xattn_W': _L0_xattn_in['W'], 'L0_xattn_b': _L0_xattn_in['b'], 'L0_ffn_weight': _L0_ffn_in['weight']}

def reference(x, ctx_1024, mask_BxSxS2_ik0, g_xattn, g_ffn, L0_xattn_W, L0_xattn_b, L0_ffn_weight):
    import jax
    import jax.numpy as jnp

    def _L0_xattn_ref(query, memories, mask, W, b):
        import jax, jax.numpy as jnp
        import numpy as np
        NEG = -1000000000.0
        q = jnp.einsum('bsd,od->bso', query, W) + b
        add_mask = (1.0 - mask.astype(q.dtype)) * NEG
        attn_logits = jnp.einsum('bqd,bkd->bqk', q, memories) + add_mask
        attn_weights = jax.nn.softmax(attn_logits, axis=-1)
        attn_outputs = jnp.einsum('bqk,bkd->bqd', attn_weights, memories)
        return attn_outputs

    def _L0_ffn_ref(x, weight):
        import jax, jax.numpy as jnp
        import numpy as np
        b_weight = jnp.sign(weight)
        return jnp.einsum('bsi,oi->bso', x, b_weight)
    x = x + jnp.tanh(g_xattn[0]) * _L0_xattn_ref(_layernorm(x, axis=-1), ctx_1024, mask_BxSxS2_ik0, L0_xattn_W, L0_xattn_b)
    x = x + jnp.tanh(g_ffn[0]) * _L0_ffn_ref(_layernorm(x, axis=-1), L0_ffn_weight)
    return x

_drawn_inputs = setup_inputs


def setup_inputs(seed=0):
    import zlib

    import numpy as np

    out = dict(_drawn_inputs(seed))
    spreads = {'L0_xattn_b': (0.0, 0.1)}
    factors = {}
    for name, (base, spread) in spreads.items():
        noise = np.random.default_rng([zlib.crc32(name.encode()), seed]).standard_normal(out[name].shape)
        drawn = base * np.exp(spread * noise) if base else spread * noise
        out[name] = jnp.asarray(drawn.astype(out[name].dtype))
    for name, factor in factors.items():
        out[name] = (out[name] * factor).astype(out[name].dtype)
    return out
```

```python
from contextlib import ExitStack

import concourse.bass as bass
from concourse import mybir

F32 = mybir.dt.float32
F32R = mybir.dt.float32r
I32 = mybir.dt.int32
ALU = mybir.AluOpType
ACT = mybir.ActivationFunctionType
AX = mybir.AxisListType

P = 128
R = 4
EPS = 1e-5
NEG = -1e9
DMA = 16


def flamingo_block(nc: bass.Bass, x: bass.AP, ctx: bass.AP, mask: bass.AP, g_xattn: bass.AP,
                   g_ffn: bass.AP, w_q: bass.AP, b_q: bass.AP, w_ffn: bass.AP, out: bass.AP):
    NB, S, D = x.shape
    K = ctx.shape[1]
    T = S // P
    C = D // P
    assert T == 2 and C == 2 and K <= P and NB % R == 0 and R * K <= 512 and T * D <= 512

    x_rows = x.rearrange("b (p j) d -> b p j d", j=T)
    out_rows = out.rearrange("b (p j) d -> b p j d", j=T)
    mask_rows = mask.rearrange("b (p j) k -> b p j k", j=T)
    ctx_keys = ctx.rearrange("b k d -> k b d")

    with ExitStack() as stack:
        def sb(name, shape, dt=F32):
            return stack.enter_context(nc.sbuf_tensor(name, shape, dt))

        def ps(name, shape):
            return stack.enter_context(nc.psum_tensor(name, shape, F32))

        def sem(name):
            return stack.enter_context(nc.semaphore(name))

        ident = sb("ident", [P, P])
        wq_raw = sb("wq_raw", [P, C, D])
        wq_c = sb("wq_c", [P, C, D])
        wf_raw = sb("wf_raw", [P, C, D])
        wf_pos = sb("wf_pos", [P, C, D])
        wf_sign = sb("wf_sign", [P, C, D])
        wf_c = sb("wf_c", [P, C, D])
        wf_t = sb("wf_t", [P, C, D], F32R)
        row_sum = sb("row_sum", [P, 2 * C])
        row_mean = sb("row_mean", [P, 2 * C])
        bq_col = sb("bq_col", [P, C])
        g_raw = sb("g_raw", [P, 2])
        g_tanh = sb("g_tanh", [P, 2])
        gate_attn = sb("gate_attn", [P, T])
        gate_ffn = sb("gate_ffn", [P, T])
        minus_half = sb("minus_half", [P, T])
        eps = sb("eps", [P, T])

        x_in = sb("x_in", [P, R, T, D])
        mask_in = sb("mask_in", [P, R, T, K], I32)
        ctx_v = sb("ctx_v", [K, R, D])
        ctx_q = sb("ctx_q", [K, R, D])
        ctx_t = sb("ctx_t", [P, C, R, K])
        m_sb = sb("m_sb", [P, C, R, K])
        nb_ctx = sb("nb_ctx", [K, R])
        xs = sb("xs", [P, 2, T, D])
        x_t = sb("x_t", [P, 2, C, S])
        l_t = sb("l_t", [K, 2, S])
        neg_mask = sb("neg_mask", [P, 2, T, K])
        neg_l = sb("neg_l", [P, 2, T, K])
        neg_max = sb("neg_max", [P, R, T])
        prob = sb("prob", [P, 2, T, K])
        prob_sum = sb("prob_sum", [P, R, T])
        recip = sb("recip", [P, R, T])
        c1 = sb("c1", [P, R, T])
        p_t = sb("p_t", [K, 2, S])
        x1 = sb("x1", [P, R, T, D])
        x1_hi = sb("x1_hi", [P, 2, C, S], F32R)
        x1_lo = sb("x1_lo", [P, 2, C, S], F32R)
        st1 = sb("st1", [P, 2, T, 6])
        mv1 = sb("mv1", [P, R, T, 2])
        ve1 = sb("ve1", [P, R, T])
        rstd1 = sb("rstd1", [P, R, T])
        st2 = sb("st2", [P, 2, T, 6])
        mv2 = sb("mv2", [P, R, T, 2])
        ve2 = sb("ve2", [P, R, T])
        rstd2 = sb("rstd2", [P, R, T])
        c2 = sb("c2", [P, R, T])
        y = sb("y", [P, R, T, D])

        xt_ps = ps("xt_ps", [P, C, S])
        ctx_ps = ps("ctx_ps", [P, 512])
        lt_ps = ps("lt_ps", [P, 512])
        row_ps = ps("row_ps", [P, 512])
        pt_ps = ps("pt_ps", [P, 512])
        pv_ps = ps("pv_ps", [P, T, D])
        x1t_ps = ps("x1t_ps", [P, C, S])
        ffn_ps = ps("ffn_ps", [P, T, D])

        const_loaded = sem("const_loaded")
        ident_ready = sem("ident_ready")
        half_ready = sem("half_ready")
        gate_ready = sem("gate_ready")
        tanh_ready = sem("tanh_ready")
        prep_step = sem("prep_step")
        wq_ready = sem("wq_ready")
        wf_ready = sem("wf_ready")
        wft_psum = sem("wft_psum")
        wft_ready = sem("wft_ready")
        x_loaded = [sem(f"x_loaded{r}") for r in range(R)]
        mask_loaded = [sem(f"mask_loaded{r}") for r in range(R)]
        ctxv_loaded = [sem(f"ctxv_loaded{r}") for r in range(R)]
        ctxq_loaded = sem("ctxq_loaded")
        y_stored = [sem(f"y_stored{r}") for r in range(R)]
        stats1_part = sem("stats1_part")
        stats1_done = sem("stats1_done")
        ve1_done = sem("ve1_done")
        rstd1_done = sem("rstd1_done")
        xs_done = sem("xs_done")
        negmask_done = sem("negmask_done")
        xt_psum = sem("xt_psum")
        xt_done = sem("xt_done")
        lt_psum = sem("lt_psum")
        lt_done = sem("lt_done")
        row_psum = sem("row_psum")
        logits_done = sem("logits_done")
        exp_done = sem("exp_done")
        pt_psum = sem("pt_psum")
        pt_done = sem("pt_done")
        recip_done = sem("recip_done")
        c1_done = sem("c1_done")
        pv_psum = sem("pv_psum")
        x1_done = sem("x1_done")
        stats2_part = sem("stats2_part")
        stats2_done = sem("stats2_done")
        ve2_done = sem("ve2_done")
        rstd2_done = sem("rstd2_done")
        c2_done = sem("c2_done")
        x1t_psum = sem("x1t_psum")
        hi_done = sem("hi_done")
        lo_done = sem("lo_done")
        ffn_psum = sem("ffn_psum")
        y_done = sem("y_done")
        ctx_psum = sem("ctx_psum")
        ctx_done = sem("ctx_done")

        def at_least(eng, s, value):
            if not isinstance(value, int) or value > 0:
                eng.wait_ge(s, value)

        def landed(t0, n):
            return t0 * (DMA // R) + DMA * (n // R + 1)

        def exists(t0, n):
            return not isinstance(t0, int) or 0 <= t0 + n < NB

        FIRST = R
        LAST = NB - R
        END = NB + 3

        def pipeline(eng, slot):
            for t in range(FIRST):
                slot(t - t % R, t % R)
            with eng.Fori(FIRST // R, LAST // R) as group:
                for r in range(R):
                    slot(group * R, r)
            for t in range(LAST, END):
                slot(t - t % R, t % R)

        block = stack.enter_context(nc.Block())

        @block.sync
        def _(sp):
            def load(t0, n):
                i = n % R
                sp.dma_start(x_in[:, i], x_rows[t0 + n]).then_inc(x_loaded[i], DMA)
                sp.dma_start(mask_in[:, i], mask_rows[t0 + n]).then_inc(mask_loaded[i], DMA)
                sp.dma_start(ctx_v[:, i], ctx_keys[:, t0 + n]).then_inc(ctxv_loaded[i], DMA)

            sp.dma_start(ctx_q[:], ctx_keys[:, 0:R]).then_inc(ctxq_loaded, DMA)
            sp.dma_start(wq_raw[:], w_q.rearrange("(c p) i -> p c i", c=C)).then_inc(const_loaded, DMA)
            sp.dma_start(x_in[:, 0], x_rows[0]).then_inc(x_loaded[0], DMA)
            sp.dma_start(bq_col[:], b_q.rearrange("(c p) -> p c", c=C),
                         allow_slow_non_contiguous=True).then_inc(const_loaded, DMA)
            sp.dma_start(g_raw[:, 0:1], g_xattn.partition_broadcast(P)).then_inc(const_loaded, DMA)
            sp.dma_start(g_raw[:, 1:2], g_ffn.partition_broadcast(P)).then_inc(const_loaded, DMA)
            sp.dma_start(wf_raw[:], w_ffn.rearrange("(c p) i -> p c i", c=C)).then_inc(const_loaded, DMA)
            sp.dma_start(mask_in[:, 0], mask_rows[0]).then_inc(mask_loaded[0], DMA)
            sp.dma_start(ctx_v[:, 0], ctx_keys[:, 0]).then_inc(ctxv_loaded[0], DMA)
            for n in range(1, R - 1):
                load(0, n)

            def slot(t0, r):
                t = t0 + r
                if r == 0 and exists(t0, R):
                    sp.wait_ge(ctx_psum, t + 2)
                    sp.dma_start(ctx_q[:], ctx_keys[:, bass.ds(t0 + R, R)]).then_inc(ctxq_loaded, DMA)
                if exists(t0, r - 3):
                    i = (r - 3) % R
                    at_least(sp, y_done, t - 2)
                    sp.dma_start(out_rows[t - 3], y[:, i]).then_inc(y_stored[i], DMA)
                if exists(t0, r + 3):
                    at_least(sp, x1_done, t)
                    at_least(sp, pv_psum, t)
                    at_least(sp, negmask_done, t)
                    load(t0, r + 3)

            pipeline(sp, slot)
            for i in range(R):
                sp.wait_ge(y_stored[i], DMA * (NB // R))

        @block.gpsimd
        def _(pool):
            pool.memset(ident[:], 0.0).then_inc(ident_ready, 1)
            pool.memset(minus_half[:], -0.5).then_inc(half_ready, 1)
            pool.memset(eps[:], EPS).then_inc(half_ready, 1)
            pool.wait_ge(ident_ready, 1)
            pool.affine_select(out=ident[:], in_=ident[:], compare_op=ALU.not_equal, fill=1.0, base=0,
                               pattern=[[-1, P]], channel_multiplier=1).then_inc(ident_ready, 1)
            pool.wait_ge(half_ready, 2)

            def add_eps(mv, ve, i, k, stats, ve_done):
                pool.wait_ge(stats, k)
                pool.tensor_tensor(ve[:, i], mv[:, i, :, 1], eps[:], ALU.add).then_inc(ve_done, 1)

            def power(ve, res, i, k, ve_done, res_done):
                pool.wait_ge(ve_done, k)
                pool.tensor_tensor(res[:, i], ve[:, i], minus_half[:], ALU.pow).then_inc(res_done, 1)

            def negmask(n):
                pool.tensor_scalar(neg_mask[:, n % 2], mask_in[:, n % R], -1.0, NEG, ALU.add,
                                   ALU.mult).then_inc(negmask_done, 1)

            add_eps(mv1, ve1, 0, 1, stats1_done, ve1_done)
            power(ve1, rstd1, 0, 1, ve1_done, rstd1_done)
            pool.wait_ge(mask_loaded[0], DMA)
            negmask(0)
            pool.wait_ge(gate_ready, 2)

            def slot(t0, r):
                t = t0 + r
                if exists(t0, r + 1):
                    at_least(pool, logits_done, t)
                    pool.wait_ge(mask_loaded[(r + 1) % R], landed(t0, r + 1))
                    add_eps(mv1, ve1, (r + 1) % R, t + 2, stats1_done, ve1_done)
                    negmask(r + 1)
                    power(ve1, rstd1, (r + 1) % R, t + 2, ve1_done, rstd1_done)
                if exists(t0, r - 2):
                    i = (r - 2) % R
                    add_eps(mv2, ve2, i, t - 1, stats2_done, ve2_done)
                    power(ve2, rstd2, i, t - 1, ve2_done, rstd2_done)
                    pool.wait_ge(rstd2_done, t - 1)
                    pool.tensor_tensor(c2[:, i], rstd2[:, i], gate_ffn[:], ALU.mult).then_inc(c2_done, 1)

            pipeline(pool, slot)

        @block.scalar
        def _(act):
            def scale_rows(t0, n):
                i = n % R
                act.wait_ge(rstd1_done, t0 + n + 1)
                act.wait_ge(x_loaded[i], landed(t0, n))
                at_least(act, xt_psum, t0 + n - 1)
                for j in range(T):
                    ins = act.activation(xs[:, n % 2, j], x_in[:, i, j], ACT.Copy,
                                         scale=rstd1[:, i, j:j + 1])
                ins.then_inc(xs_done, 1)

            def keys_step(half, count):
                act.wait_ge(ctx_psum, count)
                act.activation(ctx_t[:, :, 2 * half:2 * half + 2, :],
                               ctx_ps[:, 0:C * 2 * K].rearrange("p (c b k) -> p c b k", c=C, b=2),
                               ACT.Copy).then_inc(ctx_done, 1)

            def m_step(c, count):
                act.wait_ge(ctx_psum, count)
                if c == 0:
                    act.activation(nb_ctx[:], ctx_ps[0:K, R * K:R * K + R], ACT.Copy, scale=-1.0)
                act.activation(m_sb[:, c], ctx_ps[:, 0:R * K].rearrange("p (b k) -> p b k", b=R),
                               ACT.Copy).then_inc(ctx_done, 1)

            act.wait_ge(const_loaded, 5 * DMA)
            act.activation(g_tanh[:], g_raw[:], ACT.Tanh).then_inc(tanh_ready, 1)
            keys_step(0, 1)
            keys_step(1, 2)
            m_step(0, 3)
            scale_rows(0, 0)
            act.wait_ge(wft_psum, 1)
            act.activation(wf_t[:], ffn_ps[:], ACT.Copy).then_inc(wft_ready, 1)

            def slot(t0, r):
                t = t0 + r
                if exists(t0, r):
                    act.wait_ge(xt_psum, t + 1)
                    at_least(act, lt_psum, t - 1)
                    act.activation(x_t[:, r % 2], xt_ps[:], ACT.Copy).then_inc(xt_done, 1)
                if r == 0 and exists(t0, r):
                    m_step(1, t + 4)
                if r in (1, 2) and exists(t0, R):
                    keys_step(r - 1, t + 4)
                if exists(t0, r - 1):
                    act.wait_ge(pt_psum, t)
                    at_least(act, pv_psum, t - 2)
                    act.activation(p_t[:, (r - 1) % 2], pt_ps[0:K, 0:S], ACT.Copy).then_inc(pt_done, 1)
                if exists(t0, r - 2):
                    act.wait_ge(x1t_psum, t - 1)
                    at_least(act, ffn_psum, t - 3)
                    act.activation(x1_hi[:, r % 2], x1t_ps[:], ACT.Copy).then_inc(hi_done, 1)
                if exists(t0, r):
                    act.wait_ge(lt_psum, t + 1)
                    at_least(act, row_psum, t - 1)
                    act.activation(l_t[:, r % 2], lt_ps[0:K, 0:S], ACT.Identity, scale=-1.0,
                                   bias=nb_ctx[:, r:r + 1]).then_inc(lt_done, 1)
                if exists(t0, r + 1):
                    scale_rows(t0, r + 1)
                if r == 3 and exists(t0, R):
                    m_step(0, t + 4)
                if exists(t0, r):
                    act.wait_ge(logits_done, t + 1)
                    at_least(act, pt_psum, t - 1)
                    for j in range(T):
                        ins = act.activation(prob[:, r % 2, j], neg_l[:, r % 2, j], ACT.Exp, scale=-1.0,
                                             bias=neg_max[:, r, j:j + 1],
                                             accum_out=prob_sum[:, r, j:j + 1])
                    ins.then_inc(exp_done, 1)

            pipeline(act, slot)

        @block.vector
        def _(dve):
            def moments(src, st, i, n, part):
                for j in range(T):
                    ins = dve.bn_stats(st[:, n % 2, j], src[:, i, j])
                ins.then_inc(part, 1)

            def combine(st, mv, i, n, done):
                for j in range(T):
                    ins = dve.bn_aggr(mv[:, i, j], st[:, n % 2, j])
                ins.then_inc(done, 1)

            def stats1(n):
                dve.wait_ge(x_loaded[n], DMA)
                moments(x_in, st1, n, n, stats1_part)
                dve.wait_ge(stats1_part, n + 1)
                combine(st1, mv1, n, n, stats1_done)

            step = [0]

            def prepared(ins):
                step[0] += 1
                ins.then_inc(prep_step, 1)
                return step[0]

            dve.wait_ge(const_loaded, 5 * DMA)
            dve.wait_ge(prep_step, prepared(dve.tensor_reduce(row_sum[:, 0:C], wq_raw[:], AX.X, ALU.add)))
            dve.wait_ge(prep_step, prepared(dve.tensor_scalar(row_mean[:, 0:C], row_sum[:, 0:C], 1.0 / D,
                                                              None, ALU.mult)))
            for c in range(C):
                ins = dve.tensor_scalar(wq_c[:, c], wq_raw[:, c], row_mean[:, c:c + 1], None, ALU.subtract)
            ins.then_inc(wq_ready, 1)
            stats1(0)
            dve.wait_ge(prep_step, prepared(dve.tensor_scalar(wf_pos[:], wf_raw[:], 0.0, None, ALU.is_gt)))
            dve.wait_ge(prep_step, prepared(dve.tensor_scalar(wf_sign[:], wf_raw[:], 0.0, None, ALU.is_lt)))
            dve.wait_ge(prep_step, prepared(dve.tensor_tensor(wf_sign[:], wf_pos[:], wf_sign[:],
                                                              ALU.subtract)))
            dve.wait_ge(prep_step, prepared(dve.tensor_reduce(row_sum[:, C:2 * C], wf_sign[:], AX.X, ALU.add)))
            dve.wait_ge(prep_step, prepared(dve.tensor_scalar(row_mean[:, C:2 * C], row_sum[:, C:2 * C],
                                                              1.0 / D, None, ALU.mult)))
            for c in range(C):
                ins = dve.tensor_scalar(wf_c[:, c], wf_sign[:, c], row_mean[:, C + c:C + c + 1], None,
                                        ALU.subtract)
            ins.then_inc(wf_ready, 1)
            dve.wait_ge(tanh_ready, 1)
            for j in range(T):
                dve.tensor_copy(gate_attn[:, j:j + 1], g_tanh[:, 0:1])
                ins = dve.tensor_copy(gate_ffn[:, j:j + 1], g_tanh[:, 1:2])
                ins.then_inc(gate_ready, 1)

            def slot(t0, r):
                t = t0 + r
                if exists(t0, r - 3):
                    i = (r - 3) % R
                    dve.wait_ge(ffn_psum, t - 2)
                    dve.wait_ge(c2_done, t - 2)
                    if exists(t0, r - 7):
                        dve.wait_ge(y_stored[i], landed(t0, r - 7))
                    for j in range(T):
                        ins = dve.scalar_tensor_tensor(out=y[:, i, j], in0=ffn_ps[:, j],
                                                       scalar=c2[:, i, j:j + 1], in1=x1[:, i, j],
                                                       op0=ALU.mult, op1=ALU.add)
                    ins.then_inc(y_done, 1)
                if exists(t0, r + 1):
                    dve.wait_ge(x_loaded[(r + 1) % R], landed(t0, r + 1))
                    moments(x_in, st1, (r + 1) % R, r, stats1_part)
                if exists(t0, r - 2):
                    dve.wait_ge(x1_done, t - 1)
                    moments(x1, st2, (r - 2) % R, r, stats2_part)
                if exists(t0, r + 1):
                    dve.wait_ge(stats1_part, t + 2)
                if exists(t0, r - 1):
                    i = (r - 1) % R
                    dve.wait_ge(exp_done, t)
                    dve.reciprocal(recip[:, i], prob_sum[:, i]).then_inc(recip_done, 1)
                if exists(t0, r + 1):
                    combine(st1, mv1, (r + 1) % R, r, stats1_done)
                if exists(t0, r - 2):
                    dve.wait_ge(stats2_part, t - 1)
                    dve.wait_ge(hi_done, t - 1)
                    dve.tensor_tensor(x1_lo[:, r % 2], x1t_ps[:], x1_hi[:, r % 2].bitcast(F32),
                                      ALU.subtract).then_inc(lo_done, 1)
                    combine(st2, mv2, (r - 2) % R, r, stats2_done)
                if exists(t0, r):
                    dve.wait_ge(row_psum, t + 1)
                    dve.wait_ge(negmask_done, t + 1)
                    at_least(dve, exp_done, t - 1)
                if exists(t0, r - 1):
                    i = (r - 1) % R
                    dve.wait_ge(recip_done, t)
                    dve.tensor_tensor(c1[:, i], recip[:, i], gate_attn[:], ALU.mult).then_inc(c1_done, 1)
                if exists(t0, r):
                    for j in range(T):
                        ins = dve.tensor_tensor_reduce(out=neg_l[:, r % 2, j],
                                                       in0=row_ps[:, j * K:(j + 1) * K],
                                                       in1=neg_mask[:, r % 2, j], scale=1.0, scalar=3.0e38,
                                                       op0=ALU.add, op1=ALU.min,
                                                       accum_out=neg_max[:, r, j:j + 1])
                    ins.then_inc(logits_done, 1)
                if exists(t0, r - 1):
                    i = (r - 1) % R
                    dve.wait_ge(pv_psum, t)
                    dve.wait_ge(c1_done, t)
                    for j in range(T):
                        ins = dve.scalar_tensor_tensor(out=x1[:, i, j], in0=pv_ps[:, j],
                                                       scalar=c1[:, i, j:j + 1], in1=x_in[:, i, j],
                                                       op0=ALU.mult, op1=ALU.add)
                    ins.then_inc(x1_done, 1)

            pipeline(dve, slot)

        @block.tensor
        def _(pe):
            def keys_step(half, count):
                at_least(pe, ctx_done, count - 1)
                for c in range(C):
                    for b in range(2):
                        at = (c * 2 + b) * K
                        ins = pe.transpose(ctx_ps[:, at:at + K],
                                           ctx_q[:, 2 * half + b, c * P:(c + 1) * P], ident[0:K, 0:K])
                ins.then_inc(ctx_psum, 1)

            def m_step(c, count):
                pe.wait_ge(ctx_done, count - 1)
                if c == 0:
                    for b in range(R):
                        for o in range(C):
                            pe.matmul(ctx_ps[0:K, R * K + b:R * K + b + 1], ctx_t[:, o, b],
                                      bq_col[:, o:o + 1], start=(o == 0), stop=(o == C - 1))
                for o in range(C):
                    ins = pe.matmul(ctx_ps[:, 0:R * K], wq_c[:, o, c * P:(c + 1) * P],
                                    ctx_t[:, o].rearrange("p b k -> p (b k)"),
                                    start=(o == 0), stop=(o == C - 1))
                ins.then_inc(ctx_psum, 1)

            pe.wait_ge(ident_ready, 2)
            pe.wait_ge(ctxq_loaded, DMA)
            keys_step(0, 1)
            keys_step(1, 2)
            pe.wait_ge(const_loaded, 5 * DMA)
            pe.wait_ge(wq_ready, 1)
            m_step(0, 3)
            pe.wait_ge(wf_ready, 1)
            for i in range(C):
                for o in range(C):
                    ins = pe.transpose(ffn_ps[:, i, o * P:(o + 1) * P], wf_c[:, o, i * P:(i + 1) * P],
                                       ident[:])
            ins.then_inc(wft_psum, 1)
            pe.wait_ge(wft_ready, 1)

            def slot(t0, r):
                t = t0 + r
                if exists(t0, r):
                    pe.wait_ge(xs_done, t + 1)
                    at_least(pe, xt_done, t)
                    for c in range(C):
                        for j in range(T):
                            ins = pe.transpose(xt_ps[:, c, j * P:(j + 1) * P],
                                               xs[:, r % 2, j, c * P:(c + 1) * P], ident[:])
                    ins.then_inc(xt_psum, 1)
                if r == 0 and exists(t0, r):
                    m_step(1, t + 4)
                if r in (1, 2) and exists(t0, R):
                    pe.wait_ge(ctxq_loaded, landed(t0, R))
                    keys_step(r - 1, t + 4)
                if exists(t0, r - 1):
                    pe.wait_ge(exp_done, t)
                    at_least(pe, pt_done, t - 1)
                    for j in range(T):
                        ins = pe.transpose(pt_ps[0:K, j * P:(j + 1) * P], prob[:, (r - 1) % 2, j], ident[:])
                    ins.then_inc(pt_psum, 1)
                if exists(t0, r - 2):
                    pe.wait_ge(x1_done, t - 1)
                    at_least(pe, lo_done, t - 2)
                    for c in range(C):
                        for j in range(T):
                            ins = pe.transpose(x1t_ps[:, c, j * P:(j + 1) * P],
                                               x1[:, (r - 2) % R, j, c * P:(c + 1) * P], ident[:])
                    ins.then_inc(x1t_psum, 1)
                if exists(t0, r):
                    pe.wait_ge(xt_done, t + 1)
                    if r == 0:
                        pe.wait_ge(ctx_done, t + 4)
                    at_least(pe, lt_done, t)
                    for c in range(C):
                        ins = pe.matmul(lt_ps[0:K, 0:S], m_sb[:, c, r], x_t[:, r % 2, c],
                                        start=(c == 0), stop=(c == C - 1))
                    ins.then_inc(lt_psum, 1)
                if exists(t0, r - 1):
                    i = (r - 1) % R
                    pe.wait_ge(pt_done, t)
                    pe.wait_ge(ctxv_loaded[i], landed(t0, r - 1))
                    at_least(pe, x1_done, t - 1)
                    for j in range(T):
                        ins = pe.matmul(pv_ps[:, j], p_t[:, (r - 1) % 2, j * P:(j + 1) * P], ctx_v[:, i],
                                        start=True, stop=True)
                    ins.then_inc(pv_psum, 1)
                if exists(t0, r):
                    pe.wait_ge(lt_done, t + 1)
                    at_least(pe, logits_done, t)
                    for j in range(T):
                        ins = pe.transpose(row_ps[:, j * K:(j + 1) * K], l_t[:, r % 2, j * P:(j + 1) * P],
                                           ident[0:K, 0:K])
                    ins.then_inc(row_psum, 1)
                if r == 3 and exists(t0, R):
                    m_step(0, t + 4)
                if exists(t0, r - 2):
                    pe.wait_ge(lo_done, t - 1)
                    at_least(pe, y_done, t - 2)
                    for j in range(T):
                        for n, part in enumerate((x1_hi, x1_lo)):
                            for c in range(C):
                                ins = pe.matmul(ffn_ps[:, j], part[:, r % 2, c, j * P:(j + 1) * P],
                                                wf_t[:, c], start=(n == 0 and c == 0),
                                                stop=(n == 1 and c == C - 1))
                    ins.then_inc(ffn_psum, 1)

            pipeline(pe, slot)


_INS = ["x", "ctx_1024", "mask_BxSxS2_ik0", "g_xattn", "g_ffn", "L0_xattn_W", "L0_xattn_b", "L0_ffn_weight"]


def kernel(**inputs):
    import numpy as _np
    import concourse.bacc as _bacc
    from concourse import mybir as _mybir
    from concourse.bass_utils import run_bass_kernel_spmd as _run

    nc = _bacc.Bacc("TRN2", target_bir_lowering=False, num_devices=1)
    arrays, args = {}, []
    for name in _INS:
        a = _np.ascontiguousarray(inputs[name])
        arrays[f"in_{name}_dram"] = a
        args.append(nc.dram_tensor(f"in_{name}_dram", a.shape, _mybir.dt.from_np(a.dtype), kind="ExternalInput").ap())
    out = nc.dram_tensor("out_0_dram", inputs["x"].shape, _mybir.dt.float32, kind="ExternalOutput").ap()
    flamingo_block(nc, *args, out)
    r = _run(nc, [arrays], core_ids=[0])
    return r.results[0]["out_0_dram"]
```

```python
from contextlib import ExitStack

import concourse.bass as bass
from concourse import mybir

F32 = mybir.dt.float32
F32R = mybir.dt.float32r
I32 = mybir.dt.int32
ALU = mybir.AluOpType
ACT = mybir.ActivationFunctionType
AX = mybir.AxisListType

P = 128
R = 4
EPS = 1e-5
NEG = -1e9
DMA = 16


def flamingo_block(nc: bass.Bass, x: bass.AP, ctx: bass.AP, mask: bass.AP, g_xattn: bass.AP,
                   g_ffn: bass.AP, w_q: bass.AP, b_q: bass.AP, w_ffn: bass.AP, out: bass.AP):
    NB, S, D = x.shape
    K = ctx.shape[1]
    T = S // P
    C = D // P
    assert T == 2 and C == 2 and K <= P and NB % R == 0 and R * K <= 512 and T * D <= 512

    x_rows = x.rearrange("b (p j) d -> b p j d", j=T)
    out_rows = out.rearrange("b (p j) d -> b p j d", j=T)
    mask_rows = mask.rearrange("b (p j) k -> b p j k", j=T)
    ctx_keys = ctx.rearrange("b k d -> k b d")

    with ExitStack() as stack:
        def sb(name, shape, dt=F32):
            return stack.enter_context(nc.sbuf_tensor(name, shape, dt))

        def ps(name, shape):
            return stack.enter_context(nc.psum_tensor(name, shape, F32))

        def sem(name):
            return stack.enter_context(nc.semaphore(name))

        ident = sb("ident", [P, P])
        wq_raw = sb("wq_raw", [P, C, D])
        wq_c = sb("wq_c", [P, C, D])
        wf_raw = sb("wf_raw", [P, C, D])
        wf_pos = sb("wf_pos", [P, C, D])
        wf_sign = sb("wf_sign", [P, C, D])
        wf_c = sb("wf_c", [P, C, D])
        wf_t = sb("wf_t", [P, C, D], F32R)
        row_sum = sb("row_sum", [P, 2 * C])
        row_mean = sb("row_mean", [P, 2 * C])
        bq_col = sb("bq_col", [P, C])
        g_raw = sb("g_raw", [P, 2])
        g_tanh = sb("g_tanh", [P, 2])
        gate_attn = sb("gate_attn", [P, T])
        gate_ffn = sb("gate_ffn", [P, T])
        minus_half = sb("minus_half", [P, T])
        eps = sb("eps", [P, T])
        one = sb("one", [P, T])

        x_in = sb("x_in", [P, R, T, D])
        mask_in = sb("mask_in", [P, R, T, K], I32)
        ctx_v = sb("ctx_v", [K, R, D])
        ctx_q = sb("ctx_q", [K, R, D])
        ctx_t = sb("ctx_t", [P, C, 2, K])
        m_sb = sb("m_sb", [P, C, R, K])
        xs = sb("xs", [P, 2, T, D])
        x_t = sb("x_t", [P, 2, C, S])
        neg_mask = sb("neg_mask", [P, 2, T, K])
        neg_l = sb("neg_l", [P, 2, T, K])
        neg_max = sb("neg_max", [P, R, T])
        prob = sb("prob", [P, 2, T, K])
        prob_sum = sb("prob_sum", [P, R, T])
        recip = sb("recip", [P, R, T])
        c1 = sb("c1", [P, R, T])
        p_t = sb("p_t", [K, 2, S])
        x1 = sb("x1", [P, R, T, D])
        x1_hi = sb("x1_hi", [P, 2, C, S], F32R)
        x1_lo = sb("x1_lo", [P, 2, C, S], F32R)
        st1 = sb("st1", [P, 2, T, 6])
        mv1 = sb("mv1", [P, R, T, 2])
        ve1 = sb("ve1", [P, R, T])
        rstd1 = sb("rstd1", [P, R, T])
        mr1 = sb("mr1", [P, R, T])
        shift1 = sb("shift1", [P, R, T])
        st2 = sb("st2", [P, 2, T, 6])
        mv2 = sb("mv2", [P, R, T, 2])
        ve2 = sb("ve2", [P, R, T])
        rstd2 = sb("rstd2", [P, R, T])
        c2 = sb("c2", [P, R, T])
        ffn_scaled = sb("ffn_scaled", [P, 2, D])
        y = sb("y", [P, R, T, D])

        xt_ps = ps("xt_ps", [P, C, S])
        ctx_ps = ps("ctx_ps", [P, 512])
        l_ps = ps("l_ps", [P, 512])
        pt_ps = ps("pt_ps", [P, 512])
        pv_ps = ps("pv_ps", [P, T, D])
        x1t_ps = ps("x1t_ps", [P, C, S])
        ffn_ps = [ps(f"ffn_ps{j}", [P, 512]) for j in range(T)]

        const_loaded = sem("const_loaded")
        ident_ready = sem("ident_ready")
        half_ready = sem("half_ready")
        gate_ready = sem("gate_ready")
        tanh_ready = sem("tanh_ready")
        prep_step = sem("prep_step")
        wq_ready = sem("wq_ready")
        wf_ready = sem("wf_ready")
        wft_psum = sem("wft_psum")
        wft_ready = sem("wft_ready")
        x_loaded = [sem(f"x_loaded{r}") for r in range(R)]
        mask_loaded = [sem(f"mask_loaded{r}") for r in range(R)]
        ctxv_loaded = [sem(f"ctxv_loaded{r}") for r in range(R)]
        ctxq_loaded = [sem(f"ctxq_loaded{h}") for h in range(R // 2)]
        y_stored = [sem(f"y_stored{r}") for r in range(R)]
        stats1_part = sem("stats1_part")
        stats1_done = sem("stats1_done")
        ve1_done = sem("ve1_done")
        rstd1_done = sem("rstd1_done")
        mr1_done = sem("mr1_done")
        shift1_done = sem("shift1_done")
        xs_done = sem("xs_done")
        negmask_done = sem("negmask_done")
        xt_psum = sem("xt_psum")
        xt_done = sem("xt_done")
        l_psum = sem("l_psum")
        logits_done = sem("logits_done")
        exp_done = sem("exp_done")
        pt_psum = sem("pt_psum")
        pt_done = sem("pt_done")
        recip_done = sem("recip_done")
        c1_done = sem("c1_done")
        pv_psum = sem("pv_psum")
        x1_done = sem("x1_done")
        stats2_part = sem("stats2_part")
        stats2_done = sem("stats2_done")
        ve2_done = sem("ve2_done")
        rstd2_done = sem("rstd2_done")
        c2_done = sem("c2_done")
        x1t_psum = sem("x1t_psum")
        hi_done = sem("hi_done")
        lo_done = sem("lo_done")
        ffn_psum = sem("ffn_psum")
        ffn_scaled_done = sem("ffn_scaled_done")
        y_done = sem("y_done")
        y_last_done = sem("y_last_done")
        ctx_psum = sem("ctx_psum")
        ctx_done = sem("ctx_done")

        def at_least(eng, s, value):
            if not isinstance(value, int) or value > 0:
                eng.wait_ge(s, value)

        def landed(t0, n):
            return t0 * (DMA // R) + DMA * (n // R + 1)

        def exists(t0, n):
            return not isinstance(t0, int) or 0 <= t0 + n < NB

        FIRST = R
        LAST = NB - R
        END = NB + 3

        def pipeline(eng, slot):
            for t in range(FIRST):
                slot(t - t % R, t % R)
            with eng.Fori(FIRST // R, LAST // R) as group:
                for r in range(R):
                    slot(group * R, r)
            for t in range(LAST, END):
                slot(t - t % R, t % R)

        block = stack.enter_context(nc.Block())

        @block.sync
        def _(sp):
            def load(t0, n):
                i = n % R
                sp.dma_start(x_in[:, i], x_rows[t0 + n]).then_inc(x_loaded[i], DMA)
                sp.dma_start(mask_in[:, i], mask_rows[t0 + n]).then_inc(mask_loaded[i], DMA)
                sp.dma_start(ctx_v[:, i], ctx_keys[:, t0 + n]).then_inc(ctxv_loaded[i], DMA)

            sp.dma_start(ctx_q[:, 0:2], ctx_keys[:, 0:2]).then_inc(ctxq_loaded[0], DMA)
            sp.dma_start(wq_raw[:], w_q.rearrange("(c p) i -> p c i", c=C)).then_inc(const_loaded, DMA)
            sp.dma_start(x_in[:, 0], x_rows[0]).then_inc(x_loaded[0], DMA)
            sp.dma_start(bq_col[:], b_q.rearrange("(c p) -> p c", c=C),
                         allow_slow_non_contiguous=True).then_inc(const_loaded, DMA)
            sp.dma_start(g_raw[:, 0:1], g_xattn.partition_broadcast(P)).then_inc(const_loaded, DMA)
            sp.dma_start(g_raw[:, 1:2], g_ffn.partition_broadcast(P)).then_inc(const_loaded, DMA)
            sp.dma_start(wf_raw[:], w_ffn.rearrange("(c p) i -> p c i", c=C)).then_inc(const_loaded, DMA)
            sp.dma_start(mask_in[:, 0], mask_rows[0]).then_inc(mask_loaded[0], DMA)
            sp.dma_start(ctx_v[:, 0], ctx_keys[:, 0]).then_inc(ctxv_loaded[0], DMA)
            load(0, 1)
            sp.dma_start(ctx_q[:, 2:4], ctx_keys[:, 2:4]).then_inc(ctxq_loaded[1], DMA)
            load(0, 2)

            def slot(t0, r):
                t = t0 + r
                if r % 2 == 0 and exists(t0, r + 4):
                    sp.wait_ge(ctx_psum, 2 * t + 1)
                    sp.dma_start(ctx_q[:, r:r + 2],
                                 ctx_keys[:, bass.ds(t + 4, 2)]).then_inc(ctxq_loaded[r // 2], DMA)
                if exists(t0, r - 3):
                    i = (r - 3) % R
                    at_least(sp, y_done, t - 2)
                    at_least(sp, y_last_done, t - 2)
                    sp.dma_start(out_rows[t - 3], y[:, i]).then_inc(y_stored[i], DMA)
                if exists(t0, r + 3):
                    at_least(sp, x1_done, t)
                    at_least(sp, pv_psum, t)
                    at_least(sp, negmask_done, t)
                    load(t0, r + 3)

            pipeline(sp, slot)
            for i in range(R):
                sp.wait_ge(y_stored[i], DMA * (NB // R))

        @block.gpsimd
        def _(pool):
            pool.memset(ident[:], 0.0).then_inc(ident_ready, 1)
            pool.memset(minus_half[:], -0.5).then_inc(half_ready, 1)
            pool.memset(eps[:], EPS).then_inc(half_ready, 1)
            pool.memset(one[:], 1.0).then_inc(half_ready, 1)
            pool.wait_ge(ident_ready, 1)
            pool.affine_select(out=ident[:], in_=ident[:], compare_op=ALU.not_equal, fill=1.0, base=0,
                               pattern=[[-1, P]], channel_multiplier=1).then_inc(ident_ready, 1)
            pool.wait_ge(half_ready, 3)

            def add_eps(mv, ve, i, k, stats, ve_done):
                pool.wait_ge(stats, k)
                pool.tensor_tensor(ve[:, i], mv[:, i, :, 1], eps[:], ALU.add).then_inc(ve_done, 1)

            def power(ve, res, i, k, ve_done, res_done):
                pool.wait_ge(ve_done, k)
                pool.tensor_tensor(res[:, i], ve[:, i], minus_half[:], ALU.pow).then_inc(res_done, 1)

            def negmask(n):
                pool.tensor_scalar(neg_mask[:, n % 2], mask_in[:, n % R], -1.0, NEG, ALU.add,
                                   ALU.mult).then_inc(negmask_done, 1)

            def shift(i, k):
                pool.wait_ge(rstd1_done, k)
                pool.tensor_tensor(mr1[:, i], mv1[:, i, :, 0], rstd1[:, i], ALU.mult).then_inc(mr1_done, 1)
                pool.wait_ge(mr1_done, k)
                pool.tensor_tensor(shift1[:, i], one[:], mr1[:, i], ALU.subtract).then_inc(shift1_done, 1)

            for n in range(2):
                add_eps(mv1, ve1, n, n + 1, stats1_done, ve1_done)
                power(ve1, rstd1, n, n + 1, ve1_done, rstd1_done)
                shift(n, n + 1)
            pool.wait_ge(mask_loaded[0], DMA)
            negmask(0)
            pool.wait_ge(gate_ready, 2)

            def slot(t0, r):
                t = t0 + r
                if exists(t0, r + 1) and exists(t0, r - 1):
                    add_eps(mv1, ve1, (r + 1) % R, t + 2, stats1_done, ve1_done)
                    power(ve1, rstd1, (r + 1) % R, t + 2, ve1_done, rstd1_done)
                    shift((r + 1) % R, t + 2)
                if exists(t0, r - 3):
                    i = (r - 3) % R
                    pool.wait_ge(ffn_scaled_done, t - 2)
                    if exists(t0, r - 7):
                        pool.wait_ge(y_stored[i], landed(t0, r - 7))
                    pool.tensor_tensor(y[:, i, T - 1], ffn_scaled[:, (r - 3) % 2], x1[:, i, T - 1],
                                       ALU.add).then_inc(y_last_done, 1)
                if exists(t0, r + 1):
                    pool.wait_ge(mask_loaded[(r + 1) % R], landed(t0, r + 1))
                    at_least(pool, logits_done, t)
                if exists(t0, r - 2):
                    add_eps(mv2, ve2, (r - 2) % R, t - 1, stats2_done, ve2_done)
                if exists(t0, r + 1):
                    negmask(r + 1)
                if exists(t0, r - 2):
                    i = (r - 2) % R
                    power(ve2, rstd2, i, t - 1, ve2_done, rstd2_done)
                    pool.wait_ge(rstd2_done, t - 1)
                    pool.tensor_tensor(c2[:, i], rstd2[:, i], gate_ffn[:], ALU.mult).then_inc(c2_done, 1)

            pipeline(pool, slot)

        @block.scalar
        def _(act):
            def scale_rows(t0, n):
                i = n % R
                act.wait_ge(shift1_done, t0 + n + 1)
                act.wait_ge(x_loaded[i], landed(t0, n))
                at_least(act, xt_psum, t0 + n - 1)
                for j in range(T):
                    ins = act.activation(xs[:, n % 2, j], x_in[:, i, j], ACT.Identity,
                                         scale=rstd1[:, i, j:j + 1], bias=shift1[:, i, j:j + 1])
                ins.then_inc(xs_done, 1)

            def keys_step(count):
                act.wait_ge(ctx_psum, count)
                act.activation(ctx_t[:], ctx_ps[:, 0:C * 2 * K].rearrange("p (c b k) -> p c b k", c=C, b=2),
                               ACT.Copy).then_inc(ctx_done, 1)

            def m_step(c, pair, count):
                act.wait_ge(ctx_psum, count)
                act.activation(m_sb[:, c, 2 * pair:2 * pair + 2],
                               ctx_ps[:, 0:2 * K].rearrange("p (b k) -> p b k", b=2),
                               ACT.Copy, scale=-1.0).then_inc(ctx_done, c + 1)

            act.wait_ge(const_loaded, 5 * DMA)
            act.activation(g_tanh[:], g_raw[:], ACT.Tanh).then_inc(tanh_ready, 1)
            keys_step(1)
            m_step(0, 0, 2)
            m_step(1, 0, 4)
            scale_rows(0, 0)
            act.wait_ge(wft_psum, 1)
            for i in range(C):
                ins = act.activation(wf_t[:, i], ffn_ps[i][:, 0:D], ACT.Copy)
            ins.then_inc(wft_ready, 1)

            def slot(t0, r):
                t = t0 + r
                if exists(t0, r):
                    act.wait_ge(xt_psum, t + 1)
                    at_least(act, l_psum, t - 1)
                    act.activation(x_t[:, r % 2], xt_ps[:], ACT.Copy).then_inc(xt_done, 1)
                if r % 2 == 0 and exists(t0, r + 2):
                    keys_step(2 * t + 5)
                if r % 2 == 1 and exists(t0, r + 1):
                    m_step(1, (r // 2 + 1) % 2, 2 * t + 6)
                if exists(t0, r - 1):
                    act.wait_ge(pt_psum, t)
                    at_least(act, pv_psum, t - 2)
                    act.activation(p_t[:, (r - 1) % 2], pt_ps[0:K, 0:S], ACT.Copy).then_inc(pt_done, 1)
                if exists(t0, r - 2):
                    act.wait_ge(x1t_psum, t - 1)
                    at_least(act, ffn_psum, t - 3)
                    act.activation(x1_hi[:, r % 2], x1t_ps[:], ACT.Copy).then_inc(hi_done, 1)
                if exists(t0, r - 3):
                    act.wait_ge(c2_done, t - 2)
                    act.wait_ge(ffn_psum, t - 2)
                    at_least(act, y_last_done, t - 4)
                    act.activation(ffn_scaled[:, (r - 3) % 2], ffn_ps[T - 1][:, 0:D], ACT.Copy,
                                   scale=c2[:, (r - 3) % R, T - 1:T]).then_inc(ffn_scaled_done, 1)
                if exists(t0, r + 1):
                    scale_rows(t0, r + 1)
                if r % 2 == 0 and exists(t0, r + 2):
                    m_step(0, (r // 2 + 1) % 2, 2 * t + 6)
                if exists(t0, r):
                    act.wait_ge(logits_done, t + 1)
                    at_least(act, pt_psum, t - 1)
                    for j in range(T):
                        ins = act.activation(prob[:, r % 2, j], neg_l[:, r % 2, j], ACT.Exp, scale=-1.0,
                                             bias=neg_max[:, r, j:j + 1],
                                             accum_out=prob_sum[:, r, j:j + 1])
                    ins.then_inc(exp_done, 1)

            pipeline(act, slot)

        @block.vector
        def _(dve):
            def moments(src, st, i, n, part):
                for j in range(T):
                    ins = dve.bn_stats(st[:, n % 2, j], src[:, i, j])
                ins.then_inc(part, 1)

            def combine(st, mv, i, n, done):
                for j in range(T):
                    ins = dve.bn_aggr(mv[:, i, j], st[:, n % 2, j])
                ins.then_inc(done, 1)

            def stats1(n):
                dve.wait_ge(x_loaded[n], DMA)
                moments(x_in, st1, n, n, stats1_part)
                dve.wait_ge(stats1_part, n + 1)
                combine(st1, mv1, n, n, stats1_done)

            step = [0]

            def prepared(ins):
                step[0] += 1
                ins.then_inc(prep_step, 1)
                return step[0]

            dve.wait_ge(const_loaded, 5 * DMA)
            dve.wait_ge(prep_step, prepared(dve.tensor_reduce(row_sum[:, 0:C], wq_raw[:], AX.X, ALU.add)))
            dve.wait_ge(prep_step, prepared(dve.tensor_tensor(row_sum[:, 0:C], row_sum[:, 0:C], bq_col[:],
                                                              ALU.subtract)))
            dve.wait_ge(prep_step, prepared(dve.tensor_scalar(row_mean[:, 0:C], row_sum[:, 0:C], 1.0 / D,
                                                              None, ALU.mult)))
            for c in range(C):
                ins = dve.tensor_scalar(wq_c[:, c], wq_raw[:, c], row_mean[:, c:c + 1], None, ALU.subtract)
            ins.then_inc(wq_ready, 1)
            stats1(0)
            stats1(1)
            dve.wait_ge(prep_step, prepared(dve.tensor_scalar(wf_pos[:], wf_raw[:], 0.0, None, ALU.is_gt)))
            dve.wait_ge(prep_step, prepared(dve.tensor_scalar(wf_sign[:], wf_raw[:], 0.0, None, ALU.is_lt)))
            dve.wait_ge(prep_step, prepared(dve.tensor_tensor(wf_sign[:], wf_pos[:], wf_sign[:],
                                                              ALU.subtract)))
            dve.wait_ge(prep_step, prepared(dve.tensor_reduce(row_sum[:, C:2 * C], wf_sign[:], AX.X, ALU.add)))
            dve.wait_ge(prep_step, prepared(dve.tensor_scalar(row_mean[:, C:2 * C], row_sum[:, C:2 * C],
                                                              1.0 / D, None, ALU.mult)))
            for c in range(C):
                ins = dve.tensor_scalar(wf_c[:, c], wf_sign[:, c], row_mean[:, C + c:C + c + 1], None,
                                        ALU.subtract)
            ins.then_inc(wf_ready, 1)
            dve.wait_ge(tanh_ready, 1)
            for j in range(T):
                dve.tensor_copy(gate_attn[:, j:j + 1], g_tanh[:, 0:1])
                ins = dve.tensor_copy(gate_ffn[:, j:j + 1], g_tanh[:, 1:2])
                ins.then_inc(gate_ready, 1)

            def slot(t0, r):
                t = t0 + r
                if exists(t0, r + 1) and exists(t0, r - 1):
                    dve.wait_ge(stats1_part, t + 2)
                if exists(t0, r - 1):
                    dve.wait_ge(exp_done, t)
                    dve.reciprocal(recip[:, (r - 1) % R], prob_sum[:, (r - 1) % R]).then_inc(recip_done, 1)
                if exists(t0, r + 1) and exists(t0, r - 1):
                    combine(st1, mv1, (r + 1) % R, r + 1, stats1_done)
                if exists(t0, r - 3):
                    i = (r - 3) % R
                    dve.wait_ge(ffn_psum, t - 2)
                    dve.wait_ge(c2_done, t - 2)
                    if exists(t0, r - 7):
                        dve.wait_ge(y_stored[i], landed(t0, r - 7))
                    for j in range(T - 1):
                        ins = dve.scalar_tensor_tensor(out=y[:, i, j], in0=ffn_ps[j][:, 0:D],
                                                       scalar=c2[:, i, j:j + 1], in1=x1[:, i, j],
                                                       op0=ALU.mult, op1=ALU.add)
                    ins.then_inc(y_done, 1)
                if exists(t0, r - 2):
                    dve.wait_ge(x1_done, t - 1)
                    moments(x1, st2, (r - 2) % R, r, stats2_part)
                if exists(t0, r - 2):
                    dve.wait_ge(stats2_part, t - 1)
                    dve.wait_ge(hi_done, t - 1)
                    dve.tensor_tensor(x1_lo[:, r % 2], x1t_ps[:], x1_hi[:, r % 2].bitcast(F32),
                                      ALU.subtract).then_inc(lo_done, 1)
                    combine(st2, mv2, (r - 2) % R, r, stats2_done)
                if exists(t0, r):
                    dve.wait_ge(l_psum, t + 1)
                    dve.wait_ge(negmask_done, t + 1)
                    at_least(dve, exp_done, t - 1)
                if exists(t0, r - 1):
                    i = (r - 1) % R
                    dve.wait_ge(recip_done, t)
                    dve.tensor_tensor(c1[:, i], recip[:, i], gate_attn[:], ALU.mult).then_inc(c1_done, 1)
                if exists(t0, r):
                    for j in range(T):
                        ins = dve.tensor_tensor_reduce(out=neg_l[:, r % 2, j],
                                                       in0=l_ps[:, j * K:(j + 1) * K],
                                                       in1=neg_mask[:, r % 2, j], scale=1.0, scalar=3.0e38,
                                                       op0=ALU.add, op1=ALU.min,
                                                       accum_out=neg_max[:, r, j:j + 1])
                    ins.then_inc(logits_done, 1)
                if exists(t0, r - 1):
                    i = (r - 1) % R
                    dve.wait_ge(pv_psum, t)
                    dve.wait_ge(c1_done, t)
                    at_least(dve, y_last_done, t - 4)
                    for j in range(T):
                        ins = dve.scalar_tensor_tensor(out=x1[:, i, j], in0=pv_ps[:, j],
                                                       scalar=c1[:, i, j:j + 1], in1=x_in[:, i, j],
                                                       op0=ALU.mult, op1=ALU.add)
                    ins.then_inc(x1_done, 1)
                if exists(t0, r + 2):
                    dve.wait_ge(x_loaded[(r + 2) % R], landed(t0, r + 2))
                    moments(x_in, st1, (r + 2) % R, r, stats1_part)

            pipeline(dve, slot)

        @block.tensor
        def _(pe):
            def keys_step(pair, count):
                at_least(pe, ctx_done, count - 1)
                for c in range(C):
                    for b in range(2):
                        at = (c * 2 + b) * K
                        ins = pe.transpose(ctx_ps[:, at:at + K],
                                           ctx_q[:, 2 * pair + b, c * P:(c + 1) * P], ident[0:K, 0:K])
                ins.then_inc(ctx_psum, 1)

            def m_step(c, count):
                pe.wait_ge(ctx_done, count)
                for o in range(C):
                    ins = pe.matmul(ctx_ps[:, 0:2 * K], wq_c[:, o, c * P:(c + 1) * P],
                                    ctx_t[:, o].rearrange("p b k -> p (b k)"),
                                    start=(o == 0), stop=(o == C - 1))
                ins.then_inc(ctx_psum, c + 1)

            pe.wait_ge(ident_ready, 2)
            pe.wait_ge(ctxq_loaded[0], DMA)
            keys_step(0, 1)
            pe.wait_ge(const_loaded, 5 * DMA)
            pe.wait_ge(wq_ready, 1)
            m_step(0, 1)
            m_step(1, 2)
            pe.wait_ge(wf_ready, 1)
            for i in range(C):
                for o in range(C):
                    ins = pe.transpose(ffn_ps[i][:, o * P:(o + 1) * P], wf_c[:, o, i * P:(i + 1) * P],
                                       ident[:])
            ins.then_inc(wft_psum, 1)
            pe.wait_ge(wft_ready, 1)

            def slot(t0, r):
                t = t0 + r
                if exists(t0, r):
                    pe.wait_ge(xs_done, t + 1)
                    at_least(pe, xt_done, t)
                    for c in range(C):
                        for j in range(T):
                            ins = pe.transpose(xt_ps[:, c, j * P:(j + 1) * P],
                                               xs[:, r % 2, j, c * P:(c + 1) * P], ident[:])
                    ins.then_inc(xt_psum, 1)
                if r % 2 == 0 and exists(t0, r + 2):
                    pe.wait_ge(ctxq_loaded[(r // 2 + 1) % 2], landed(t0, r + 2))
                    keys_step((r // 2 + 1) % 2, 2 * t + 5)
                if r % 2 == 1 and exists(t0, r + 1):
                    m_step(1, 2 * t + 4)
                if exists(t0, r - 1):
                    pe.wait_ge(exp_done, t)
                    at_least(pe, pt_done, t - 1)
                    for j in range(T):
                        ins = pe.transpose(pt_ps[0:K, j * P:(j + 1) * P], prob[:, (r - 1) % 2, j], ident[:])
                    ins.then_inc(pt_psum, 1)
                if exists(t0, r - 2):
                    pe.wait_ge(x1_done, t - 1)
                    at_least(pe, lo_done, t - 2)
                    for c in range(C):
                        for j in range(T):
                            ins = pe.transpose(x1t_ps[:, c, j * P:(j + 1) * P],
                                               x1[:, (r - 2) % R, j, c * P:(c + 1) * P], ident[:])
                    ins.then_inc(x1t_psum, 1)
                if exists(t0, r):
                    pe.wait_ge(xt_done, t + 1)
                    if r % 2 == 0:
                        pe.wait_ge(ctx_done, 2 * t + 4)
                    at_least(pe, logits_done, t)
                    for j in range(T):
                        for c in range(C):
                            ins = pe.matmul(l_ps[:, j * K:(j + 1) * K],
                                            x_t[:, r % 2, c, j * P:(j + 1) * P], m_sb[:, c, r],
                                            start=(c == 0), stop=(c == C - 1))
                    ins.then_inc(l_psum, 1)
                if exists(t0, r - 1):
                    i = (r - 1) % R
                    pe.wait_ge(pt_done, t)
                    pe.wait_ge(ctxv_loaded[i], landed(t0, r - 1))
                    at_least(pe, x1_done, t - 1)
                    for j in range(T):
                        ins = pe.matmul(pv_ps[:, j], p_t[:, (r - 1) % 2, j * P:(j + 1) * P], ctx_v[:, i],
                                        start=True, stop=True)
                    ins.then_inc(pv_psum, 1)
                if r % 2 == 0 and exists(t0, r + 2):
                    m_step(0, 2 * t + 5)
                if exists(t0, r - 2):
                    pe.wait_ge(lo_done, t - 1)
                    at_least(pe, y_done, t - 2)
                    at_least(pe, ffn_scaled_done, t - 2)
                    for j in range(T):
                        for n, part in enumerate((x1_hi, x1_lo)):
                            for c in range(C):
                                ins = pe.matmul(ffn_ps[j][:, 0:D], part[:, r % 2, c, j * P:(j + 1) * P],
                                                wf_t[:, c], start=(n == 0 and c == 0),
                                                stop=(n == 1 and c == C - 1))
                    ins.then_inc(ffn_psum, 1)

            pipeline(pe, slot)


_INS = ["x", "ctx_1024", "mask_BxSxS2_ik0", "g_xattn", "g_ffn", "L0_xattn_W", "L0_xattn_b", "L0_ffn_weight"]


def kernel(**inputs):
    import numpy as _np
    import concourse.bacc as _bacc
    from concourse import mybir as _mybir
    from concourse.bass_utils import run_bass_kernel_spmd as _run

    nc = _bacc.Bacc("TRN2", target_bir_lowering=False, num_devices=1)
    arrays, args = {}, []
    for name in _INS:
        a = _np.ascontiguousarray(inputs[name])
        arrays[f"in_{name}_dram"] = a
        args.append(nc.dram_tensor(f"in_{name}_dram", a.shape, _mybir.dt.from_np(a.dtype), kind="ExternalInput").ap())
    out = nc.dram_tensor("out_0_dram", inputs["x"].shape, _mybir.dt.float32, kind="ExternalOutput").ap()
    flamingo_block(nc, *args, out)
    r = _run(nc, [arrays], core_ids=[0])
    return r.results[0]["out_0_dram"]
```

```python
from contextlib import ExitStack

import concourse.bass as bass
from concourse import mybir

F32 = mybir.dt.float32
F32R = mybir.dt.float32r
I32 = mybir.dt.int32
ALU = mybir.AluOpType
ACT = mybir.ActivationFunctionType
AX = mybir.AxisListType

P = 128
N = 8
R = 4
AHEAD = 5
EPS = 1e-5
NEG = -1e9
DMA = 16


def flamingo_block(nc: bass.Bass, x: bass.AP, ctx: bass.AP, mask: bass.AP, g_xattn: bass.AP,
                   g_ffn: bass.AP, w_q: bass.AP, b_q: bass.AP, w_ffn: bass.AP, out: bass.AP):
    NB, S, D = x.shape
    K = ctx.shape[1]
    T = S // P
    C = D // P
    assert T == 2 and C == 2 and K <= P and NB % N == 0 and 2 * C * K <= 512 and T * D <= 512

    x_rows = x.rearrange("b (p j) d -> b p j d", j=T)
    out_rows = out.rearrange("b (p j) d -> b p j d", j=T)
    mask_pairs = mask.rearrange("b (p j) k -> p b j k", j=T)
    ctx_keys = ctx.rearrange("b k d -> k b d")

    with ExitStack() as stack:
        def sb(name, shape, dt=F32):
            return stack.enter_context(nc.sbuf_tensor(name, shape, dt))

        def ps(name, shape):
            return stack.enter_context(nc.psum_tensor(name, shape, F32))

        def sem(name):
            return stack.enter_context(nc.semaphore(name))

        ident = sb("ident", [P, P])
        wq_raw = sb("wq_raw", [P, C, D])
        wq_c = sb("wq_c", [P, C, D])
        wf_raw = sb("wf_raw", [P, C, D])
        wf_neg = sb("wf_neg", [P, C, D])
        wf_sign = sb("wf_sign", [P, C, D])
        wf_c = sb("wf_c", [P, C, D])
        wf_t = sb("wf_t", [P, C, D], F32R)
        row_sum = sb("row_sum", [P, 2 * C])
        row_mean = sb("row_mean", [P, 2 * C])
        bq_col = sb("bq_col", [P, C])
        g_raw = sb("g_raw", [P, 2])
        g_tanh = sb("g_tanh", [P, 2])
        gate_attn = sb("gate_attn", [P, T])
        gate_ffn = sb("gate_ffn", [P, T])
        minus_half = sb("minus_half", [P, T])
        eps = sb("eps", [P, T])
        one = sb("one", [P, T])

        x_in = sb("x_in", [P, N, T, D])
        mask_in = sb("mask_in", [P, N, T, K], I32)
        ctx_v = sb("ctx_v", [K, N, D])
        ctx_t = sb("ctx_t", [P, C, 2, K])
        m_sb = sb("m_sb", [P, C, R, K])
        xs = sb("xs", [P, 2, T, D])
        x_t = sb("x_t", [P, 2, C, S])
        neg_mask = sb("neg_mask", [P, 2, T, K])
        neg_l = sb("neg_l", [P, 2, T, K])
        neg_max = sb("neg_max", [P, R, T])
        prob = sb("prob", [P, 2, T, K])
        prob_sum = sb("prob_sum", [P, R, T])
        recip = sb("recip", [P, R, T])
        c1 = sb("c1", [P, R, T])
        p_t = sb("p_t", [K, 2, S])
        x1 = sb("x1", [P, R, T, D])
        x1_hi = sb("x1_hi", [P, 2, C, S], F32R)
        x1_lo = sb("x1_lo", [P, 2, C, S], F32R)
        st1 = sb("st1", [P, 2, T, 6])
        mv1 = sb("mv1", [P, R, T, 2])
        ve1 = sb("ve1", [P, R, T])
        rstd1 = sb("rstd1", [P, R, T])
        mr1 = sb("mr1", [P, R, T])
        shift1 = sb("shift1", [P, R, T])
        st2 = sb("st2", [P, 2, T, 6])
        mv2 = sb("mv2", [P, R, T, 2])
        ve2 = sb("ve2", [P, R, T])
        rstd2 = sb("rstd2", [P, R, T])
        c2 = sb("c2", [P, R, T])
        ffn_scaled = sb("ffn_scaled", [P, 2, D])
        y = sb("y", [P, R, T, D])

        xt_ps = ps("xt_ps", [P, C, S])
        ctx_ps = ps("ctx_ps", [P, 512])
        l_ps = ps("l_ps", [P, 512])
        pt_ps = ps("pt_ps", [P, 512])
        pv_ps = ps("pv_ps", [P, T, D])
        x1t_ps = ps("x1t_ps", [P, C, S])
        ffn_ps = [ps(f"ffn_ps{j}", [P, 512]) for j in range(T)]

        wq_loaded = sem("wq_loaded")
        gates_loaded = sem("gates_loaded")
        wf_loaded = sem("wf_loaded")
        ident_ready = sem("ident_ready")
        half_ready = sem("half_ready")
        gate_ready = sem("gate_ready")
        tanh_ready = sem("tanh_ready")
        prep_step = sem("prep_step")
        wq_ready = sem("wq_ready")
        wf_ready = sem("wf_ready")
        wft_psum = sem("wft_psum")
        wft_ready = sem("wft_ready")
        x_loaded = [sem(f"x_loaded{r}") for r in range(N)]
        mask_loaded = [sem(f"mask_loaded{h}") for h in range(N // 2)]
        ctx_loaded = [sem(f"ctx_loaded{h}") for h in range(N // 2)]
        y_stored = [sem(f"y_stored{r}") for r in range(R)]
        stats1_part = sem("stats1_part")
        stats1_done = sem("stats1_done")
        ve1_done = sem("ve1_done")
        rstd1_done = sem("rstd1_done")
        mr1_done = sem("mr1_done")
        shift1_done = sem("shift1_done")
        xs_done = sem("xs_done")
        negmask_done = sem("negmask_done")
        xt_psum = sem("xt_psum")
        xt_done = sem("xt_done")
        l_psum = sem("l_psum")
        logits_done = sem("logits_done")
        exp_done = sem("exp_done")
        pt_psum = sem("pt_psum")
        pt_done = sem("pt_done")
        recip_done = sem("recip_done")
        c1_done = sem("c1_done")
        pv_psum = sem("pv_psum")
        x1_done = sem("x1_done")
        stats2_part = sem("stats2_part")
        stats2_done = sem("stats2_done")
        ve2_done = sem("ve2_done")
        rstd2_done = sem("rstd2_done")
        c2_done = sem("c2_done")
        x1t_psum = sem("x1t_psum")
        hi_done = sem("hi_done")
        lo_done = sem("lo_done")
        ffn_psum = sem("ffn_psum")
        ffn_scaled_done = sem("ffn_scaled_done")
        y_done = sem("y_done")
        y_last_done = sem("y_last_done")
        ctx_psum = sem("ctx_psum")
        ctx_done = sem("ctx_done")

        def at_least(eng, s, value):
            if not isinstance(value, int) or value > 0:
                eng.wait_ge(s, value)

        def landed(t0, n, ring=N):
            return t0 * (DMA // ring) + DMA * (n // ring + 1)

        def exists(t0, n):
            return not isinstance(t0, int) or 0 <= t0 + n < NB

        FIRST = N
        LAST = NB - N
        END = NB + 3

        def pipeline(eng, slot, after={}):
            for t in range(FIRST):
                slot(t - t % N, t % N)
                if t in after:
                    after[t]()
            with eng.Fori(FIRST // N, LAST // N) as group:
                for r in range(N):
                    slot(group * N, r)
            for t in range(LAST, END):
                slot(t - t % N, t % N)

        block = stack.enter_context(nc.Block())

        @block.sync
        def _(sp):
            def load_x(t0, n):
                sp.dma_start(x_in[:, n % N], x_rows[t0 + n]).then_inc(x_loaded[n % N], DMA)

            def load_mask(t0, n):
                i = n % N
                sp.dma_start(mask_in[:, i:i + 2],
                             mask_pairs[:, bass.ds(t0 + n, 2)]).then_inc(mask_loaded[i // 2], DMA)

            def load_ctx(t0, n):
                i = n % N
                sp.dma_start(ctx_v[:, i:i + 2],
                             ctx_keys[:, bass.ds(t0 + n, 2)]).then_inc(ctx_loaded[i // 2], DMA)

            load_x(0, 0)
            sp.dma_start(wq_raw[:], w_q.rearrange("(c p) i -> p c i", c=C)).then_inc(wq_loaded, DMA)
            sp.dma_start(bq_col[:], b_q.rearrange("(c p) -> p c", c=C),
                         allow_slow_non_contiguous=True).then_inc(wq_loaded, DMA)
            load_ctx(0, 0)
            load_x(0, 1)
            sp.dma_start(g_raw[:, 0:1], g_xattn.partition_broadcast(P)).then_inc(gates_loaded, DMA)
            sp.dma_start(g_raw[:, 1:2], g_ffn.partition_broadcast(P)).then_inc(gates_loaded, DMA)
            load_mask(0, 0)
            load_x(0, 2)
            sp.dma_start(wf_raw[:], w_ffn.rearrange("(c p) i -> p c i", c=C)).then_inc(wf_loaded, DMA)
            load_ctx(0, 2)
            load_x(0, 3)
            load_mask(0, 2)
            load_x(0, 4)

            def slot(t0, r):
                t = t0 + r
                if exists(t0, r + AHEAD):
                    at_least(sp, x1_done, t - 2)
                    load_x(t0, r + AHEAD)
                if r % 2 == 0 and exists(t0, r + 4):
                    at_least(sp, pv_psum, t - 2)
                    at_least(sp, negmask_done, t - 2)
                    load_ctx(t0, r + 4)
                    load_mask(t0, r + 4)
                if exists(t0, r - 3):
                    i = (r - 3) % R
                    at_least(sp, y_done, t - 2)
                    at_least(sp, y_last_done, t - 2)
                    sp.dma_start(out_rows[t - 3], y[:, i]).then_inc(y_stored[i], DMA)

            pipeline(sp, slot)
            for i in range(R):
                sp.wait_ge(y_stored[i], DMA * (NB // R))

        @block.gpsimd
        def _(pool):
            pool.memset(ident[:], 0.0).then_inc(ident_ready, 1)
            pool.memset(minus_half[:], -0.5).then_inc(half_ready, 1)
            pool.memset(eps[:], EPS).then_inc(half_ready, 1)
            pool.memset(one[:], 1.0).then_inc(half_ready, 1)
            pool.wait_ge(ident_ready, 1)
            pool.affine_select(out=ident[:], in_=ident[:], compare_op=ALU.not_equal, fill=1.0, base=0,
                               pattern=[[-1, P]], channel_multiplier=1).then_inc(ident_ready, 1)
            pool.wait_ge(half_ready, 3)

            def add_eps(mv, ve, i, k, stats, ve_done):
                pool.wait_ge(stats, k)
                pool.tensor_tensor(ve[:, i], mv[:, i, :, 1], eps[:], ALU.add).then_inc(ve_done, 1)

            def power(ve, res, i, k, ve_done, res_done):
                pool.wait_ge(ve_done, k)
                pool.tensor_tensor(res[:, i], ve[:, i], minus_half[:], ALU.pow).then_inc(res_done, 1)

            def negmask(n):
                pool.tensor_scalar(neg_mask[:, n % 2], mask_in[:, n % N], -1.0, NEG, ALU.add,
                                   ALU.mult).then_inc(negmask_done, 1)

            def shift(i, k):
                pool.wait_ge(rstd1_done, k)
                pool.tensor_tensor(mr1[:, i], mv1[:, i, :, 0], rstd1[:, i], ALU.mult).then_inc(mr1_done, 1)
                pool.wait_ge(mr1_done, k)
                pool.tensor_tensor(shift1[:, i], one[:], mr1[:, i], ALU.subtract).then_inc(shift1_done, 1)

            def norm1(n):
                add_eps(mv1, ve1, n, n + 1, stats1_done, ve1_done)
                power(ve1, rstd1, n, n + 1, ve1_done, rstd1_done)
                shift(n, n + 1)

            norm1(0)
            norm1(1)
            pool.wait_ge(mask_loaded[0], DMA)
            negmask(0)
            norm1(2)
            pool.wait_ge(gate_ready, 2)

            def slot(t0, r):
                t = t0 + r
                if exists(t0, r + 3):
                    add_eps(mv1, ve1, (r + 3) % R, t + 4, stats1_done, ve1_done)
                    power(ve1, rstd1, (r + 3) % R, t + 4, ve1_done, rstd1_done)
                    shift((r + 3) % R, t + 4)
                if exists(t0, r - 3):
                    i = (r - 3) % R
                    pool.wait_ge(ffn_scaled_done, t - 2)
                    if exists(t0, r - 7):
                        pool.wait_ge(y_stored[i], landed(t0, r - 7, R))
                    pool.tensor_tensor(y[:, i, T - 1], ffn_scaled[:, (r - 3) % 2], x1[:, i, T - 1],
                                       ALU.add).then_inc(y_last_done, 1)
                if exists(t0, r - 2):
                    i = (r - 2) % R
                    add_eps(mv2, ve2, i, t - 1, stats2_done, ve2_done)
                    power(ve2, rstd2, i, t - 1, ve2_done, rstd2_done)
                if exists(t0, r + 1):
                    pool.wait_ge(mask_loaded[(r + 1) % N // 2], landed(t0, r + 1))
                    at_least(pool, logits_done, t)
                if exists(t0, r - 2):
                    pool.wait_ge(rstd2_done, t - 1)
                    pool.tensor_tensor(c2[:, i], rstd2[:, i], gate_ffn[:], ALU.mult).then_inc(c2_done, 1)
                if exists(t0, r + 1):
                    negmask(r + 1)

            pipeline(pool, slot)

        @block.scalar
        def _(act):
            def scale_rows(t0, n, j):
                if j == 0:
                    act.wait_ge(shift1_done, t0 + n + 1)
                    act.wait_ge(x_loaded[n % N], landed(t0, n))
                    at_least(act, xt_psum, t0 + n - 1)
                act.activation(xs[:, n % 2, j], x_in[:, n % N, j], ACT.Identity,
                               scale=rstd1[:, n % R, j:j + 1],
                               bias=shift1[:, n % R, j:j + 1]).then_inc(xs_done, 1)

            def keys_step(count):
                act.wait_ge(ctx_psum, count)
                act.activation(ctx_t[:], ctx_ps[:, 0:C * 2 * K].rearrange("p (c b k) -> p c b k", c=C, b=2),
                               ACT.Copy).then_inc(ctx_done, 1)

            def m_step(c, pair, count):
                act.wait_ge(ctx_psum, count)
                act.activation(m_sb[:, c, 2 * pair:2 * pair + 2],
                               ctx_ps[:, 0:2 * K].rearrange("p (b k) -> p b k", b=2),
                               ACT.Copy, scale=-1.0).then_inc(ctx_done, c + 1)

            keys_step(1)
            for j in range(T):
                scale_rows(0, 0, j)
            act.wait_ge(gates_loaded, 2 * DMA)
            act.activation(g_tanh[:], g_raw[:], ACT.Tanh).then_inc(tanh_ready, 1)
            m_step(0, 0, 2)

            def ffn_weights():
                act.wait_ge(wft_psum, 1)
                for i in range(C):
                    ins = act.activation(wf_t[:, i], ffn_ps[i][:, 0:D], ACT.Copy)
                ins.then_inc(wft_ready, 1)

            def transposed_x(t0, n):
                act.wait_ge(xt_psum, t0 + n + 1)
                at_least(act, l_psum, t0 + n - 1)
                act.activation(x_t[:, n % 2], xt_ps[:], ACT.Copy).then_inc(xt_done, 1)

            transposed_x(0, 0)
            m_step(1, 0, 4)
            for j in range(T):
                scale_rows(0, 1, j)

            def slot(t0, r):
                t = t0 + r
                if exists(t0, r - 1):
                    act.wait_ge(pt_psum, t)
                    at_least(act, pv_psum, t - 2)
                    act.activation(p_t[:, (r - 1) % 2], pt_ps[0:K, 0:S], ACT.Copy).then_inc(pt_done, 1)
                if r % 2 == 0 and exists(t0, r + 2):
                    keys_step(2 * t + 5)
                if exists(t0, r - 3):
                    act.wait_ge(c2_done, t - 2)
                    act.wait_ge(ffn_psum, t - 2)
                    at_least(act, y_last_done, t - 4)
                    act.activation(ffn_scaled[:, (r - 3) % 2], ffn_ps[T - 1][:, 0:D], ACT.Copy,
                                   scale=c2[:, (r - 3) % R, T - 1:T]).then_inc(ffn_scaled_done, 1)
                if exists(t0, r + 2):
                    scale_rows(t0, r + 2, 0)
                if exists(t0, r - 2):
                    act.wait_ge(x1t_psum, t - 1)
                    at_least(act, ffn_psum, t - 3)
                    act.activation(x1_hi[:, r % 2], x1t_ps[:], ACT.Copy).then_inc(hi_done, 1)
                if exists(t0, r):
                    act.wait_ge(logits_done, t + 1)
                    at_least(act, pt_psum, t - 1)
                    for j in range(T):
                        ins = act.activation(prob[:, r % 2, j], neg_l[:, r % 2, j], ACT.Exp, scale=-1.0,
                                             bias=neg_max[:, r % R, j:j + 1],
                                             accum_out=prob_sum[:, r % R, j:j + 1])
                    ins.then_inc(exp_done, 1)
                if r % 2 == 0 and exists(t0, r + 2):
                    m_step(0, (r // 2 + 1) % 2, 2 * t + 6)
                if r % 2 == 1 and exists(t0, r + 1):
                    m_step(1, (r // 2 + 1) % 2, 2 * t + 6)
                if exists(t0, r + 1):
                    transposed_x(t0, r + 1)
                if exists(t0, r + 2):
                    scale_rows(t0, r + 2, 1)

            pipeline(act, slot, {1: ffn_weights})

        @block.vector
        def _(dve):
            def moments(src, st, i, n, part):
                for j in range(T):
                    ins = dve.bn_stats(st[:, n % 2, j], src[:, i, j])
                ins.then_inc(part, 1)

            def combine(st, mv, i, n, done):
                for j in range(T):
                    ins = dve.bn_aggr(mv[:, i, j], st[:, n % 2, j])
                ins.then_inc(done, 1)

            def stats1(n):
                dve.wait_ge(x_loaded[n], DMA)
                moments(x_in, st1, n, n, stats1_part)
                dve.wait_ge(stats1_part, n + 1)
                combine(st1, mv1, n, n, stats1_done)

            step = [0]

            def prepared(ins):
                step[0] += 1
                ins.then_inc(prep_step, 1)
                return step[0]

            stats1(0)
            dve.wait_ge(wq_loaded, 2 * DMA)
            dve.wait_ge(prep_step, prepared(dve.tensor_reduce(row_sum[:, 0:C], wq_raw[:], AX.X, ALU.add)))
            dve.wait_ge(prep_step, prepared(dve.tensor_tensor(row_sum[:, 0:C], row_sum[:, 0:C], bq_col[:],
                                                              ALU.subtract)))
            dve.wait_ge(prep_step, prepared(dve.tensor_scalar(row_mean[:, 0:C], row_sum[:, 0:C], 1.0 / D,
                                                              None, ALU.mult)))
            for c in range(C):
                ins = dve.tensor_scalar(wq_c[:, c], wq_raw[:, c], row_mean[:, c:c + 1], None, ALU.subtract)
            ins.then_inc(wq_ready, 1)
            stats1(1)
            dve.wait_ge(tanh_ready, 1)
            for j in range(T):
                dve.tensor_copy(gate_attn[:, j:j + 1], g_tanh[:, 0:1])
                ins = dve.tensor_copy(gate_ffn[:, j:j + 1], g_tanh[:, 1:2])
                ins.then_inc(gate_ready, 1)
            stats1(2)
            dve.wait_ge(wf_loaded, DMA)
            dve.wait_ge(prep_step, prepared(dve.tensor_scalar(wf_neg[:], wf_raw[:], 0.0, None, ALU.is_lt)))
            dve.wait_ge(prep_step, prepared(dve.scalar_tensor_tensor(out=wf_sign[:], in0=wf_raw[:], scalar=0.0,
                                                                     in1=wf_neg[:], op0=ALU.is_gt,
                                                                     op1=ALU.subtract)))
            dve.wait_ge(x_loaded[3], DMA)
            moments(x_in, st1, 3, 3, stats1_part)

            def centre_sign():
                dve.wait_ge(prep_step, prepared(dve.tensor_reduce(row_sum[:, C:2 * C], wf_sign[:], AX.X, ALU.add)))
                dve.wait_ge(prep_step, prepared(dve.tensor_scalar(row_mean[:, C:2 * C], row_sum[:, C:2 * C],
                                                                  1.0 / D, None, ALU.mult)))
                for c in range(C):
                    ins = dve.tensor_scalar(wf_c[:, c], wf_sign[:, c], row_mean[:, C + c:C + c + 1], None,
                                            ALU.subtract)
                ins.then_inc(wf_ready, 1)

            def slot(t0, r):
                t = t0 + r
                if exists(t0, r + 3):
                    dve.wait_ge(stats1_part, t + 4)
                if exists(t0, r - 2):
                    dve.wait_ge(x1_done, t - 1)
                    moments(x1, st2, (r - 2) % R, r, stats2_part)
                if exists(t0, r + 3):
                    combine(st1, mv1, (r + 3) % R, r + 3, stats1_done)
                if exists(t0, r - 1):
                    dve.wait_ge(exp_done, t)
                    dve.reciprocal(recip[:, (r - 1) % R], prob_sum[:, (r - 1) % R]).then_inc(recip_done, 1)
                if exists(t0, r - 2):
                    dve.wait_ge(stats2_part, t - 1)
                if exists(t0, r - 3):
                    i = (r - 3) % R
                    dve.wait_ge(ffn_psum, t - 2)
                    dve.wait_ge(c2_done, t - 2)
                    if exists(t0, r - 7):
                        dve.wait_ge(y_stored[i], landed(t0, r - 7, R))
                    for j in range(T - 1):
                        ins = dve.scalar_tensor_tensor(out=y[:, i, j], in0=ffn_ps[j][:, 0:D],
                                                       scalar=c2[:, i, j:j + 1], in1=x1[:, i, j],
                                                       op0=ALU.mult, op1=ALU.add)
                    ins.then_inc(y_done, 1)
                if exists(t0, r - 2):
                    combine(st2, mv2, (r - 2) % R, r, stats2_done)
                if exists(t0, r):
                    dve.wait_ge(l_psum, t + 1)
                    dve.wait_ge(negmask_done, t + 1)
                    at_least(dve, exp_done, t - 1)
                if exists(t0, r - 1):
                    i = (r - 1) % R
                    dve.wait_ge(recip_done, t)
                    dve.tensor_tensor(c1[:, i], recip[:, i], gate_attn[:], ALU.mult).then_inc(c1_done, 1)
                if exists(t0, r):
                    for j in range(T):
                        ins = dve.tensor_tensor_reduce(out=neg_l[:, r % 2, j],
                                                       in0=l_ps[:, j * K:(j + 1) * K],
                                                       in1=neg_mask[:, r % 2, j], scale=1.0, scalar=3.0e38,
                                                       op0=ALU.add, op1=ALU.min,
                                                       accum_out=neg_max[:, r % R, j:j + 1])
                    ins.then_inc(logits_done, 1)
                if exists(t0, r - 2):
                    dve.wait_ge(hi_done, t - 1)
                    dve.tensor_tensor(x1_lo[:, r % 2], x1t_ps[:], x1_hi[:, r % 2].bitcast(F32),
                                      ALU.subtract).then_inc(lo_done, 1)
                if exists(t0, r - 1):
                    i = (r - 1) % R
                    dve.wait_ge(pv_psum, t)
                    dve.wait_ge(c1_done, t)
                    at_least(dve, y_last_done, t - 4)
                    for j in range(T):
                        ins = dve.scalar_tensor_tensor(out=x1[:, i, j], in0=pv_ps[:, j],
                                                       scalar=c1[:, i, j:j + 1],
                                                       in1=x_in[:, (r - 1) % N, j],
                                                       op0=ALU.mult, op1=ALU.add)
                    ins.then_inc(x1_done, 1)
                if exists(t0, r + 4):
                    dve.wait_ge(x_loaded[(r + 4) % N], landed(t0, r + 4))
                    moments(x_in, st1, (r + 4) % N, r, stats1_part)

            pipeline(dve, slot, {0: centre_sign})

        @block.tensor
        def _(pe):
            def keys_step(n, count):
                at_least(pe, ctx_done, count - 1)
                for c in range(C):
                    for b in range(2):
                        at = (c * 2 + b) * K
                        ins = pe.transpose(ctx_ps[:, at:at + K],
                                           ctx_v[:, n + b, c * P:(c + 1) * P], ident[0:K, 0:K])
                ins.then_inc(ctx_psum, 1)

            def m_step(c, count):
                pe.wait_ge(ctx_done, count)
                for o in range(C):
                    ins = pe.matmul(ctx_ps[:, 0:2 * K], wq_c[:, o, c * P:(c + 1) * P],
                                    ctx_t[:, o].rearrange("p b k -> p (b k)"),
                                    start=(o == 0), stop=(o == C - 1))
                ins.then_inc(ctx_psum, c + 1)

            def warm_up(n):
                for _ in range(n):
                    pe.transpose(l_ps[:, 0:P], ident[:], ident[:])

            pe.wait_ge(ident_ready, 2)
            warm_up(16)
            pe.wait_ge(ctx_loaded[0], DMA)
            keys_step(0, 1)
            warm_up(5)
            pe.wait_ge(wq_ready, 1)
            m_step(0, 1)

            def ffn_weights():
                pe.wait_ge(wf_ready, 1)
                for i in range(C):
                    for o in range(C):
                        ins = pe.transpose(ffn_ps[i][:, o * P:(o + 1) * P], wf_c[:, o, i * P:(i + 1) * P],
                                           ident[:])
                ins.then_inc(wft_psum, 1)

            def transpose_x(t0, n):
                pe.wait_ge(xs_done, T * (t0 + n + 1))
                at_least(pe, xt_done, t0 + n)
                for c in range(C):
                    for j in range(T):
                        ins = pe.transpose(xt_ps[:, c, j * P:(j + 1) * P],
                                           xs[:, n % 2, j, c * P:(c + 1) * P], ident[:])
                ins.then_inc(xt_psum, 1)

            transpose_x(0, 0)
            m_step(1, 2)

            def slot(t0, r):
                t = t0 + r
                if exists(t0, r - 1):
                    pe.wait_ge(exp_done, t)
                    at_least(pe, pt_done, t - 1)
                    for j in range(T):
                        ins = pe.transpose(pt_ps[0:K, j * P:(j + 1) * P], prob[:, (r - 1) % 2, j], ident[:])
                    ins.then_inc(pt_psum, 1)
                if r % 2 == 0 and exists(t0, r + 2):
                    pe.wait_ge(ctx_loaded[(r + 2) % N // 2], landed(t0, r + 2))
                    keys_step((r + 2) % N, 2 * t + 5)
                if exists(t0, r):
                    pe.wait_ge(xt_done, t + 1)
                    if r % 2 == 0:
                        pe.wait_ge(ctx_done, 2 * t + 4)
                    at_least(pe, logits_done, t)
                if exists(t0, r - 2):
                    pe.wait_ge(x1_done, t - 1)
                    at_least(pe, lo_done, t - 2)
                for j in range(T):
                    for c in range(C):
                        last = (j, c) == (T - 1, C - 1)
                        if exists(t0, r):
                            ins = pe.matmul(l_ps[:, j * K:(j + 1) * K],
                                            x_t[:, r % 2, c, j * P:(j + 1) * P], m_sb[:, c, r % R],
                                            start=(c == 0), stop=(c == C - 1))
                            if last:
                                ins.then_inc(l_psum, 1)
                        if exists(t0, r - 2):
                            ins = pe.transpose(x1t_ps[:, c, j * P:(j + 1) * P],
                                               x1[:, (r - 2) % R, j, c * P:(c + 1) * P], ident[:])
                            if last:
                                ins.then_inc(x1t_psum, 1)
                if exists(t0, r - 1):
                    i = (r - 1) % N
                    pe.wait_ge(pt_done, t)
                    pe.wait_ge(ctx_loaded[i // 2], landed(t0, r - 1))
                    at_least(pe, x1_done, t - 1)
                    for j in range(T):
                        ins = pe.matmul(pv_ps[:, j], p_t[:, (r - 1) % 2, j * P:(j + 1) * P], ctx_v[:, i],
                                        start=True, stop=True)
                    ins.then_inc(pv_psum, 1)
                if r % 2 == 0 and exists(t0, r + 2):
                    m_step(0, 2 * t + 5)
                if r % 2 == 1 and exists(t0, r + 1):
                    m_step(1, 2 * t + 4)
                if exists(t0, r + 1):
                    transpose_x(t0, r + 1)
                if exists(t0, r - 2):
                    pe.wait_ge(lo_done, t - 1)
                    if isinstance(t, int) and t == 2:
                        pe.wait_ge(wft_ready, 1)
                    at_least(pe, y_done, t - 2)
                    at_least(pe, ffn_scaled_done, t - 2)
                    for j in range(T):
                        for n, part in enumerate((x1_hi, x1_lo)):
                            for c in range(C):
                                ins = pe.matmul(ffn_ps[j][:, 0:D], part[:, r % 2, c, j * P:(j + 1) * P],
                                                wf_t[:, c], start=(n == 0 and c == 0),
                                                stop=(n == 1 and c == C - 1))
                    ins.then_inc(ffn_psum, 1)

            pipeline(pe, slot, {1: ffn_weights})


_INS = ["x", "ctx_1024", "mask_BxSxS2_ik0", "g_xattn", "g_ffn", "L0_xattn_W", "L0_xattn_b", "L0_ffn_weight"]


def kernel(**inputs):
    import numpy as _np
    import concourse.bacc as _bacc
    from concourse import mybir as _mybir
    from concourse.bass_utils import run_bass_kernel_spmd as _run

    nc = _bacc.Bacc("TRN2", target_bir_lowering=False, num_devices=1)
    arrays, args = {}, []
    for name in _INS:
        a = _np.ascontiguousarray(inputs[name])
        arrays[f"in_{name}_dram"] = a
        args.append(nc.dram_tensor(f"in_{name}_dram", a.shape, _mybir.dt.from_np(a.dtype), kind="ExternalInput").ap())
    out = nc.dram_tensor("out_0_dram", inputs["x"].shape, _mybir.dt.float32, kind="ExternalOutput").ap()
    flamingo_block(nc, *args, out)
    r = _run(nc, [arrays], core_ids=[0])
    return r.results[0]["out_0_dram"]
```
